# Optimizing a Trainium2 kernel written in Bass

```python
import numpy as np
import jax
import jax.numpy as jnp

def _softmax(x, axis=-1):
    return jax.nn.softmax(x, axis=axis)
def _gelu(x):
    return jax.nn.gelu(x, approximate=True)
def _silu(x):
    return jax.nn.silu(x)
def _sigmoid(x):
    return jax.nn.sigmoid(x)
def _layernorm(x, axis=-1, eps=1e-5):
    m = jnp.mean(x, axis=axis, keepdims=True)
    v = jnp.var(x, axis=axis, keepdims=True)
    return (x - m) / jnp.sqrt(v + eps)
def _scatter_add(tgt, idx, src, axis=0):
    return tgt.at[idx].add(src)
def _segment_sum(src, seg, n):
    return jax.ops.segment_sum(src, seg, n)

kernel_name = 'mk_conv_preact_d1_conv_nchw384_624409'

def setup_inputs(seed: int = 0):
    np.random.seed(seed)
    _w = jnp.asarray
    def _rec_inputs():
        import jax
        import jax.numpy as jnp
        _gk = jax.random.key(seed)
        x = -0.0001476 + 0.9999 * jax.random.normal(jax.random.fold_in(_gk, 1), (32, 384, 56, 56), jnp.float32)
        return x
    x = _rec_inputs()
    def _L0_conv_setup():
        import jax, jax.numpy as jnp
        import numpy as np
        B, C, H, W = (32, 384, 56, 56)
        key = jax.random.key(seed)
        k1, k2, k3 = jax.random.split(key, 3)
        x = jax.random.normal(k1, (B, C, H, W), dtype=jnp.float32)
        weight = jax.random.normal(k2, (C, 1, H, 1), dtype=jnp.float32) * 0.02
        bias = jax.random.normal(k3, (C,), dtype=jnp.float32)
        return {'x': x, 'weight': weight, 'bias': bias}
    _L0_conv_all = _L0_conv_setup()
    _L0_conv_in = {k: v for k, v in _L0_conv_all.items() if k in ('weight', 'bias', )}
    del _L0_conv_all

    return {
        "x": x,
        "L0_conv_weight": _L0_conv_in["weight"],
        "L0_conv_bias": _L0_conv_in["bias"],
    }

def reference(x, L0_conv_weight, L0_conv_bias):
    import jax
    import jax.numpy as jnp
    def _L0_conv_ref(x, weight, bias):
        import jax, jax.numpy as jnp
        import numpy as np
        B, C, H, W = (32, 384, 56, 56)
        x_cat = jnp.concatenate([x, x[:, :, :-1, :]], axis=2)
        out = jax.lax.conv_general_dilated(x_cat, weight, window_strides=(1, 1), padding='VALID', dimension_numbers=('NCHW', 'OIHW', 'NCHW'), feature_group_count=x.shape[1])
        return out + bias[None, :, None, None]

    def _gn(v, G=32, eps=1e-5):
        B_, C_, H_, W_ = v.shape
        g = v.reshape(B_, G, C_ // G, H_, W_)
        m = jnp.mean(g, axis=(2, 3, 4), keepdims=True)
        s = jnp.var(g, axis=(2, 3, 4), keepdims=True)
        return ((g - m) / jnp.sqrt(s + eps)).reshape(v.shape)

    def _ln_c(v, eps=1e-6):
        m = jnp.mean(v, axis=1, keepdims=True)
        s = jnp.var(v, axis=1, keepdims=True)
        return (v - m) / jnp.sqrt(s + eps)

    def _ln_t(v, eps=1e-5):
        m = jnp.mean(v, axis=-1, keepdims=True)
        s = jnp.var(v, axis=-1, keepdims=True)
        return (v - m) / jnp.sqrt(s + eps)

    def _to_tokens(v):
        B_, C_, H_, W_ = v.shape
        return v.reshape(B_, C_, H_ * W_).transpose(0, 2, 1)
    def _from_tokens(t, like):
        B_, C_, H_, W_ = like.shape
        return t.transpose(0, 2, 1).reshape(B_, C_, H_, W_)

    x = x + _L0_conv_ref(_gn(x), L0_conv_weight, L0_conv_bias)
    return x


_drawn_inputs = setup_inputs


def setup_inputs(seed=0):
    import zlib

    import numpy as np

    out = dict(_drawn_inputs(seed))
    spreads = {}
    factors = {}
    for name, (base, spread) in spreads.items():
        noise = np.random.default_rng([zlib.crc32(name.encode()), seed]).standard_normal(out[name].shape)
        drawn = base * np.exp(spread * noise) if base else spread * noise
        out[name] = jnp.asarray(drawn.astype(out[name].dtype))
    for name, factor in factors.items():
        out[name] = (out[name] * factor).astype(out[name].dtype)
    return out
```

```python
from contextlib import ExitStack

import concourse.bass as bass
from concourse import mybir

ALU = mybir.AluOpType
ACT = mybir.ActivationFunctionType
F32 = mybir.dt.float32

B, C, H, W = 32, 384, 56, 56
GROUPS = 32
CG = C // GROUPS
EPS = 1e-5

PAR = 2
P = PAR * H
PAIRS = CG // PAR
BU = 8
QUARTERS = B // BU
UNITS = GROUPS * QUARTERS
ROW = PAIRS * W
FREE = BU * ROW
N = BU * W
COUNT = CG * H * W
TAPS = 2 * H

LEAD_LOAD = 7
LEAD_STATS = 4
LEAD_REDUCE = 3
LEAD_COEF = 2
LEAD_NORM = 1

XS = 8
NS = 2
RS = 4
BODY = 8
TURNS = UNITS // BODY
ACT_PAIRS = (0,)


def build(nc, x, taps, bias, out):
    with ExitStack() as ctx:
        def sb(name, shape):
            return ctx.enter_context(nc.sbuf_tensor(name, shape, F32))

        def psum(name, shape):
            return ctx.enter_context(nc.psum_tensor(name, shape, F32))

        def sem(name):
            return ctx.enter_context(nc.semaphore(name))

        xt = sb("xt", [P, XS, FREE])
        xn = sb("xn", [P, NS, FREE])
        circ = sb("circ", [P, 2, PAIRS, P])
        runs = sb("runs", [P, 2, H * PAIRS])
        bias_all = sb("bias_all", [P, GROUPS * PAIRS])
        bias_g = sb("bias_g", [P, 2, PAIRS])
        neg_avg = sb("neg_avg", [P, P])
        avg = sb("avg", [P, P])
        ident = sb("ident", [P, P])
        eps = sb("eps", [P, 1])
        warm = sb("warm", [P, 1])
        zeros = sb("zeros", [P, 1])
        half_count = sb("half_count", [P, BU, 2])
        minus_half = sb("minus_half", [P, BU])
        three_halves = sb("three_halves", [P, BU])
        st = sb("st", [P, RS, BU, 6])
        msum = sb("msum", [P, RS, BU])
        nmean = sb("nmean", [P, RS, BU])
        dev = sb("dev", [P, BU, 2])
        m2 = sb("m2", [P, RS, BU])
        var = sb("var", [P, RS, BU])
        std = sb("std", [P, RS, BU])
        r0 = sb("r0", [P, RS, BU])
        newt = sb("newt", [P, BU])
        rstd = sb("rstd", [P, RS, BU])
        shift = sb("shift", [P, RS, BU])

        conv = [psum(f"conv{p}", [P, 512]) for p in range(PAIRS)]
        p_mean = psum("p_mean", [P, 512])
        p_var = psum("p_var", [P, 512])

        x_loaded = [sem(f"x_loaded{s}") for s in range(XS)]
        out_stored = [sem(f"out_stored{s}") for s in range(XS)]
        taps_loaded = [sem(f"taps_loaded{s}") for s in range(2)]
        bias_loaded = sem("bias_loaded")
        consts_set = sem("consts_set")
        pool_link = sem("pool_link")
        circ_ready = sem("circ_ready")
        stats_ready = sem("stats_ready")
        msum_ready = sem("msum_ready")
        mean_ready = sem("mean_ready")
        nmean_ready = sem("nmean_ready")
        m2_ready = sem("m2_ready")
        var_ready = sem("var_ready")
        std_ready = sem("std_ready")
        r0_ready = sem("r0_ready")
        coef_ready = sem("coef_ready")
        norm_ready = sem("norm_ready")
        conv_ready = sem("conv_ready")
        taken = [sem(f"taken{p}") for p in range(PAIRS)]

        def unit_x(slot):
            return xt[:, slot, :].rearrange("k (b f) -> k b f", b=BU)

        def pair_x(slot, p):
            return xt[:, slot, :].rearrange("k (b p w) -> k b p w", b=BU, p=PAIRS)[:, :, p, :]

        def steps(step, engine):
            for j in range(BODY):
                step(0, j)
            with engine.Fori(1, TURNS - 1) as turn:
                for j in range(BODY):
                    step(turn * BODY, j)
            for j in range(BODY):
                step((TURNS - 1) * BODY, j)

        def wait_reuse(engine, semaphore, value):
            if not isinstance(value, int) or value > 0:
                engine.wait_ge(semaphore, value)

        def there(base, j):
            return not isinstance(base, int) or base + j < UNITS

        def turn_of(base, j):
            if isinstance(base, int):
                return (base + j) // XS
            return base // BODY + j // XS

        block = ctx.enter_context(nc.Block())

        @block.sync
        def _(sp):
            def load_taps(group, s):
                for par in range(PAR):
                    src = taps[group, par]
                    src = bass.AP(tensor=src.tensor, offset=src.offset, ap=[[PAIRS, H], [1, H * PAIRS]])
                    sp.dma_start(runs[par * H:(par + 1) * H, s, :], src).then_inc(taps_loaded[s], 16)

            def load(unit, slot):
                sp.dma_start(xt[:, slot, :], x[unit]).then_inc(x_loaded[slot], 16)

            load(0, 0)
            load_taps(0, 0)
            for par in range(PAR):
                sp.dma_start(bias_all[par * H:(par + 1) * H, :],
                             bias[par:par + 1, :].broadcast_to([H, GROUPS * PAIRS])
                             ).then_inc(bias_loaded, 16)
            load(1, 1)
            load_taps(1, 1)
            for n in range(2, LEAD_LOAD):
                load(n, n)

            def step(base, j):
                if j % QUARTERS == 0 and there(base, j + 2 * QUARTERS):
                    group = base // QUARTERS + j // QUARTERS
                    sp.wait_ge(circ_ready, group + 1)
                    load_taps(group + 2, (j // QUARTERS) % 2)
                for p in range(PAIRS):
                    sp.wait_ge(taken[p], base + (j + 1))
                sp.dma_start(out[base + j], xt[:, j % XS, :]).then_inc(out_stored[j % XS], 16)
                if there(base, j + LEAD_LOAD):
                    slot = (j + LEAD_LOAD) % XS
                    wait_reuse(sp, out_stored[slot], turn_of(base, j + LEAD_LOAD) * 16)
                    load(base + (j + LEAD_LOAD), slot)

            steps(step, sp)
            for s in range(XS):
                sp.wait_ge(out_stored[s], 16 * (UNITS // XS))

        @block.gpsimd
        def _(pool):
            nc.gpsimd.memset(neg_avg[:], -1.0 / (2 * P)).then_inc(consts_set, 1)
            nc.gpsimd.memset(avg[:], 1.0 / COUNT).then_inc(consts_set, 1)
            nc.gpsimd.memset(eps[:], EPS).then_inc(consts_set, 1)
            nc.gpsimd.memset(zeros[:], 0.0).then_inc(consts_set, 1)
            nc.gpsimd.memset(half_count[:], ROW / 2).then_inc(consts_set, 1)
            nc.gpsimd.memset(minus_half[:], -0.5).then_inc(consts_set, 1)
            nc.gpsimd.memset(three_halves[:], 1.5).then_inc(consts_set, 1)
            nc.gpsimd.memset(circ[:], 0.0).then_inc(consts_set, 1)
            nc.gpsimd.memset(ident[:], 0.0).then_inc(consts_set, 1)
            pool.wait_ge(consts_set, 9)
            nc.gpsimd.affine_select(out=ident[:], in_=ident[:], compare_op=ALU.not_equal, fill=1.0, base=0,
                                    pattern=[[-1, P]], channel_multiplier=1).then_inc(consts_set, 1)

            def lay_out(group, s, landed, at):
                def zero(like):
                    return zeros[0:like.shape[0], 0:1].rearrange("k (a b) -> k a b", b=1).broadcast_to(like.shape)

                def copy(dst, src):
                    return nc.gpsimd.tensor_tensor(dst, src, zero(src), ALU.add)

                fw = runs[:, s, :].rearrange("k (i p) -> k p i", p=PAIRS)[:, :, ::-1]
                pool.wait_ge(taps_loaded[s], landed)
                copy(circ[0:H, s, :, 0:H], fw[0:H]).then_inc(pool_link, 1)
                copy(circ[:, s, :, H:P], fw).then_inc(pool_link, 1)
                nc.gpsimd.tensor_tensor(bias_g[:, s, :], bias_all[:, bass.ds(group * PAIRS, PAIRS)],
                                        zeros[:, 0:1].broadcast_to([P, PAIRS]), ALU.add).then_inc(pool_link, 1)
                pool.wait_ge(pool_link, at + 3)
                upper = circ[0:H, s, :, H:P]
                nc.gpsimd.tensor_tensor(upper, zero(upper), zero(upper), ALU.add).then_inc(circ_ready, 1)

            LAY = 3
            SQ = 4
            NW = 5

            def add_means(n, s):
                pool.wait_ge(stats_ready, n + 1)
                nc.gpsimd.tensor_tensor(msum[:, s, :], st[:, s, :, 1], st[:, s, :, 4], ALU.add).then_inc(msum_ready, 1)

            def squares(n, s, at):
                pool.wait_ge(nmean_ready, n + 1)
                halves = st[:, s, :, :].rearrange("k b (e f) -> k b e f", e=2)
                nm = nmean[:, s, :].rearrange("k (b o) -> k b o", o=1).broadcast_to([P, BU, 2])
                nc.gpsimd.tensor_tensor(dev[:], halves[:, :, :, 1], nm, ALU.add).then_inc(pool_link, 1)
                pool.wait_ge(pool_link, at + 1)
                nc.gpsimd.tensor_tensor(dev[:], dev[:], dev[:], ALU.mult).then_inc(pool_link, 1)
                pool.wait_ge(pool_link, at + 2)
                nc.gpsimd.tensor_tensor(dev[:], dev[:], half_count[:], ALU.mult).then_inc(pool_link, 1)
                pool.wait_ge(pool_link, at + 3)
                nc.gpsimd.tensor_tensor(dev[:], dev[:], halves[:, :, :, 2], ALU.add).then_inc(pool_link, 1)
                pool.wait_ge(pool_link, at + 4)
                nc.gpsimd.tensor_tensor(m2[:, s, :], dev[:, :, 0], dev[:, :, 1], ALU.add).then_inc(m2_ready, 1)

            def newton(n, s, at):
                pool.wait_ge(r0_ready, n + 1)
                nc.gpsimd.tensor_tensor(newt[:], r0[:, s, :], r0[:, s, :], ALU.mult).then_inc(pool_link, 1)
                pool.wait_ge(pool_link, at + 1)
                nc.gpsimd.tensor_tensor(newt[:], newt[:], var[:, s, :], ALU.mult).then_inc(pool_link, 1)
                pool.wait_ge(pool_link, at + 2)
                nc.gpsimd.tensor_tensor(newt[:], newt[:], minus_half[:], ALU.mult).then_inc(pool_link, 1)
                pool.wait_ge(pool_link, at + 3)
                nc.gpsimd.tensor_tensor(newt[:], newt[:], three_halves[:], ALU.add).then_inc(pool_link, 1)
                pool.wait_ge(pool_link, at + 4)
                nc.gpsimd.tensor_tensor(rstd[:, s, :], newt[:], r0[:, s, :], ALU.mult).then_inc(pool_link, 1)
                pool.wait_ge(pool_link, at + 5)
                nc.gpsimd.tensor_tensor(shift[:, s, :], nmean[:, s, :], rstd[:, s, :], ALU.mult).then_inc(coef_ready, 1)

            pool.wait_ge(bias_loaded, 32)
            lay_out(0, 0, 32, 0)
            at = LAY
            for n in range(LEAD_REDUCE):
                add_means(n, n)
                squares(n, n, at)
                at += SQ
                if n < LEAD_COEF:
                    newton(n, n, at)
                    at += NW
            per_step = SQ + NW
            per_turn = BODY * per_step + (BODY // QUARTERS) * LAY
            start = at

            def step(base, j):
                at = start + base // BODY * per_turn + (j * per_step + (j + QUARTERS - 2) // QUARTERS * LAY)
                if isinstance(base, int):
                    at -= sum(SQ * (base + k + LEAD_REDUCE >= UNITS) + NW * (base + k + LEAD_COEF >= UNITS)
                              for k in range(j))
                if there(base, j + LEAD_REDUCE):
                    add_means(base + (j + LEAD_REDUCE), (j + LEAD_REDUCE) % RS)
                    squares(base + (j + LEAD_REDUCE), (j + LEAD_REDUCE) % RS, at)
                    at = at + SQ
                if there(base, j + LEAD_COEF):
                    newton(base + (j + LEAD_COEF), (j + LEAD_COEF) % RS, at)
                    at = at + NW
                if j % QUARTERS == 1 and there(base, j + QUARTERS):
                    group = base // QUARTERS + (j // QUARTERS + 1)
                    s = (j // QUARTERS + 1) % 2
                    for p in range(PAIRS):
                        wait_reuse(pool, taken[p], base + (j - 1))
                    landed = (base // BODY + (j // QUARTERS + 1) // 2) * 32 + 32
                    lay_out(group, s, landed, at)

            steps(step, pool)

        @block.vector
        def _(dve):
            def stats(base, j, b0, b1):
                n, s = base + j, j % XS
                if b0 == 0:
                    dve.wait_ge(x_loaded[s], turn_of(base, j) * 16 + 16)
                    wait_reuse(dve, m2_ready, n + (1 - RS))
                for b in range(b0, b1):
                    ins = nc.vector.bn_stats(st[:, j % RS, b, :], unit_x(s)[:, b, :])
                if b1 == BU:
                    ins.then_inc(stats_ready, 1)

            def invert(n, s):
                dve.wait_ge(std_ready, n + 1)
                nc.vector.reciprocal(r0[:, s, :], std[:, s, :]).then_inc(r0_ready, 1)

            def take(base, j, p):
                dve.wait_ge(conv_ready, (base + j) * PAIRS + (p + 1))
                nc.vector.scalar_tensor_tensor(
                    out=pair_x(j % XS, p), in0=conv[p][:, 0:N].rearrange("k (b w) -> k b w", b=BU),
                    scalar=bias_g[:, j // QUARTERS % 2, p:p + 1], in1=pair_x(j % XS, p),
                    op0=ALU.add, op1=ALU.add).then_inc(taken[p], 1)

            for n in range(LEAD_STATS):
                stats(0, n, 0, BU)
                if 1 <= n < 1 + LEAD_COEF:
                    invert(n - 1, n - 1)

            dve_pairs = [p for p in range(PAIRS) if p not in ACT_PAIRS]
            cuts = [round(k * BU / len(dve_pairs)) for k in range(len(dve_pairs) + 1)]

            def step(base, j):
                for k, p in enumerate(dve_pairs):
                    if there(base, j + LEAD_STATS):
                        stats(base, j + LEAD_STATS, cuts[k], cuts[k + 1])
                    if k == 1 and there(base, j + LEAD_COEF):
                        invert(base + (j + LEAD_COEF), (j + LEAD_COEF) % RS)
                    take(base, j, p)

            steps(step, dve)

        @block.scalar
        def _(act):
            def negmean(n, s):
                act.wait_ge(mean_ready, n + 1)
                nc.scalar.copy(nmean[:, s, :], p_mean[:, s * BU:(s + 1) * BU]).then_inc(nmean_ready, 1)

            def root(n, s):
                act.wait_ge(var_ready, n + 1)
                src = p_var[:, s * BU:(s + 1) * BU]
                nc.scalar.activation(var[:, s, :], src, ACT.Identity, bias=eps[:, 0:1])
                nc.scalar.activation(std[:, s, :], src, ACT.Sqrt, bias=eps[:, 0:1]).then_inc(std_ready, 1)

            def normalize(base, j, b0, b1):
                n = base + j
                if b0 == 0:
                    act.wait_ge(coef_ready, n + 1)
                    wait_reuse(act, conv_ready, (n + (1 - NS)) * PAIRS)
                dst = xn[:, j % NS, :].rearrange("k (b f) -> k b f", b=BU)
                for b in range(b0, b1):
                    ins = nc.scalar.activation(dst[:, b, :], unit_x(j % XS)[:, b, :], ACT.Identity,
                                               scale=rstd[:, j % RS, b:b + 1], bias=shift[:, j % RS, b:b + 1])
                if b1 == BU:
                    ins.then_inc(norm_ready, 1)

            def take(base, j, p):
                act.wait_ge(conv_ready, (base + j) * PAIRS + (p + 1))
                nc.scalar.activation(pair_x(j % XS, p), conv[p][:, 0:N].rearrange("k (b w) -> k b w", b=BU),
                                     ACT.Identity, bias=bias_g[:, j // QUARTERS % 2, p:p + 1]).then_inc(taken[p], 1)

            act.wait_ge(consts_set, 10)
            nc.scalar.activation(warm[:], eps[:], ACT.Sqrt)
            negmean(0, 0)
            root(0, 0)
            negmean(1, 1)
            normalize(0, 0, 0, BU // 4)
            root(1, 1)
            normalize(0, 0, BU // 4, 3 * BU // 4)
            negmean(2, 2)
            normalize(0, 0, 3 * BU // 4, BU)

            def step(base, j):
                if there(base, j + LEAD_COEF):
                    root(base + (j + LEAD_COEF), (j + LEAD_COEF) % RS)
                if there(base, j + LEAD_NORM):
                    normalize(base, j + LEAD_NORM, 0, 3)
                if there(base, j + LEAD_REDUCE):
                    negmean(base + (j + LEAD_REDUCE), (j + LEAD_REDUCE) % RS)
                for p in ACT_PAIRS:
                    take(base, j, p)
                if there(base, j + LEAD_NORM):
                    normalize(base, j + LEAD_NORM, 3, BU)

            steps(step, act)

        @block.tensor
        def _(pe):
            def mean(n, s):
                pe.wait_ge(msum_ready, n + 1)
                nc.tensor.matmul(p_mean[:, s * BU:(s + 1) * BU], neg_avg[:], msum[:, s, :],
                                 start=True, stop=True).then_inc(mean_ready, 1)

            def variance(n, s):
                pe.wait_ge(m2_ready, n + 1)
                nc.tensor.matmul(p_var[:, s * BU:(s + 1) * BU], avg[:], m2[:, s, :],
                                 start=True, stop=True).then_inc(var_ready, 1)

            def convolve(base, j, p):
                if p == 0:
                    pe.wait_ge(norm_ready, base + (j + 1))
                    if j % QUARTERS == 0:
                        pe.wait_ge(circ_ready, base // QUARTERS + (j // QUARTERS + 1))
                wait_reuse(pe, taken[p], base + j)
                src = xn[:, j % NS, :].rearrange("k (b p w) -> k b p w", b=BU, p=PAIRS)[:, :, p, :]
                dst = conv[p][:, 0:N]
                alone = p not in ACT_PAIRS
                ins = nc.tensor.matmul(dst, circ[:, j // QUARTERS % 2, p, :], src, start=True, stop=alone)
                if not alone:
                    ins = nc.tensor.matmul(dst, ident[:], pair_x(j % XS, p), start=False, stop=True)
                ins.then_inc(conv_ready, 1)

            pe.wait_ge(consts_set, 10)
            for n in range(LEAD_REDUCE):
                mean(n, n)
                variance(n, n)

            def step(base, j):
                convolve(base, j, 0)
                if there(base, j + LEAD_REDUCE):
                    mean(base + (j + LEAD_REDUCE), (j + LEAD_REDUCE) % RS)
                for p in range(1, PAIRS - 1):
                    convolve(base, j, p)
                if there(base, j + LEAD_REDUCE):
                    variance(base + (j + LEAD_REDUCE), (j + LEAD_REDUCE) % RS)
                convolve(base, j, PAIRS - 1)

            steps(step, pe)


def kernel(x, L0_conv_weight, L0_conv_bias):
    import numpy as np
    import concourse.bacc as bacc
    from concourse.bass_utils import run_bass_kernel_spmd

    x = np.asarray(x)
    xs = x.reshape(QUARTERS, BU, GROUPS, PAIRS, PAR, H, W).transpose(2, 0, 4, 5, 1, 3, 6)
    xs = np.ascontiguousarray(xs).reshape(UNITS, P, FREE)
    w = np.asarray(L0_conv_weight).reshape(GROUPS, PAIRS, PAR, H).transpose(0, 2, 3, 1)
    ws = np.ascontiguousarray(np.take(w, (np.arange(TAPS) + 1) % H, axis=2))
    bs = np.ascontiguousarray(np.asarray(L0_conv_bias).reshape(GROUPS * PAIRS, PAR).T)

    nc = bacc.Bacc("TRN2", target_bir_lowering=False, num_devices=1)
    arrays = {"x": xs, "taps": ws, "bias": bs}
    aps = [nc.dram_tensor(k, a.shape, F32, kind="ExternalInput").ap() for k, a in arrays.items()]
    out = nc.dram_tensor("out", (UNITS, P, FREE), F32, kind="ExternalOutput").ap()
    build(nc, *aps, out)
    got = run_bass_kernel_spmd(nc, [arrays], core_ids=[0]).results[0]["out"]
    got = got.reshape(GROUPS, QUARTERS, PAR, H, BU, PAIRS, W).transpose(1, 4, 0, 5, 2, 3, 6)
    return np.ascontiguousarray(got).reshape(B, C, H, W)
```
